# Optimizing a Trainium2 kernel written in Bass

```python
import numpy as np
import jax
import jax.numpy as jnp

def _softmax(x, axis=-1):
    return jax.nn.softmax(x, axis=axis)
def _gelu(x):
    return jax.nn.gelu(x, approximate=True)
def _silu(x):
    return jax.nn.silu(x)
def _sigmoid(x):
    return jax.nn.sigmoid(x)
def _layernorm(x, axis=-1, eps=1e-5):
    m = jnp.mean(x, axis=axis, keepdims=True)
    v = jnp.var(x, axis=axis, keepdims=True)
    return (x - m) / jnp.sqrt(v + eps)
def _scatter_add(tgt, idx, src, axis=0):
    return tgt.at[idx].add(src)
def _segment_sum(src, seg, n):
    return jax.ops.segment_sum(src, seg, n)

kernel_name = 'mk_adj_resnorm_d1_adj_1024_8e1f95'

def setup_inputs(seed: int = 0):
    np.random.seed(seed)
    _w = jnp.asarray
    def _rec_inputs():
        import jax
        import jax.numpy as jnp
        _gk = jax.random.key(seed)
        x = -0.0002928 + 1 * jax.random.normal(jax.random.fold_in(_gk, 1), (16, 1024, 1024), jnp.float32)
        _a = jax.random.bernoulli(jax.random.fold_in(_gk, 2), 0.03125, (16, 1024, 1024))
        _a = jnp.logical_or(_a, jnp.swapaxes(_a, -1, -2))
        _a = jnp.logical_or(_a, jnp.eye(1024, dtype=bool))
        adj = _a.astype(jnp.int32)
        return x, adj
    x, adj = _rec_inputs()
    def _L0_gnn_setup():
        import jax, jax.numpy as jnp
        import numpy as np
        NEG_INF = -9000000000000000.0
        ALPHA = 0.2
        H, F = (16, 64)
        key = jax.random.key(seed)
        k1, k2, k3, k4, k5 = jax.random.split(key, 5)
        B, N, D = (8, 512, 1024)
        h = jax.random.normal(k1, (B, N, D), dtype=jnp.float32)
        adj = jax.random.randint(k2, (B, N, N), 0, 2, dtype=jnp.int32)
        adj_weight = jax.random.uniform(k3, (B, N, N), dtype=jnp.float32)
        W = jax.random.normal(k4, (1, D, D), dtype=jnp.float32) * (1.414 * (6.0 / (2 * D)) ** 0.5)
        a = jax.random.normal(k5, (1, H, 2 * F, 1), dtype=jnp.float32) * 0.1
        return {'h': h, 'adj': adj, 'adj_weight': adj_weight, 'W': W, 'a': a}
    _L0_gnn_all = _L0_gnn_setup()
    _L0_gnn_in = {k: v for k, v in _L0_gnn_all.items() if k in ('W', 'a', )}
    del _L0_gnn_all

    return {
        "x": x,
        "adj": adj,
        "L0_gnn_W": _L0_gnn_in["W"],
        "L0_gnn_a": _L0_gnn_in["a"],
    }

def reference(x, adj, L0_gnn_W, L0_gnn_a):
    import jax
    import jax.numpy as jnp
    def _L0_gnn_ref(h, adj, adj_weight, W, a):
        import jax, jax.numpy as jnp
        import numpy as np
        NEG_INF = -9000000000000000.0
        ALPHA = 0.2
        H, F = (16, 64)
        B, N, D = h.shape
        Wh = jnp.matmul(h, W)
        Wh = Wh.reshape(B, N, H, F).transpose(0, 2, 1, 3)
        Wh1 = jnp.matmul(Wh, a[:, :, :F, :])
        Wh2 = jnp.matmul(Wh, a[:, :, F:, :])
        e = jax.nn.leaky_relu(Wh1 + Wh2, negative_slope=ALPHA)
        mask = (adj == 0)[:, None, :, :]
        att = jnp.where(mask, NEG_INF, e)
        att = jax.nn.softmax(att, axis=-1)
        att = att * adj_weight[:, None, :, :]
        h_prime = jnp.matmul(att, Wh)
        h_prime = h_prime.transpose(0, 2, 1, 3).reshape(B, N, H * F)
        return jax.nn.elu(h_prime)

    x = _layernorm(x + _L0_gnn_ref(x, adj, adj, L0_gnn_W, L0_gnn_a), axis=-1)
    return x


_drawn_inputs = setup_inputs


def setup_inputs(seed=0):
    import zlib

    import numpy as np

    out = dict(_drawn_inputs(seed))
    spreads = {}
    factors = {}
    for name, (base, spread) in spreads.items():
        noise = np.random.default_rng([zlib.crc32(name.encode()), seed]).standard_normal(out[name].shape)
        drawn = base * np.exp(spread * noise) if base else spread * noise
        out[name] = jnp.asarray(drawn.astype(out[name].dtype))
    for name, factor in factors.items():
        out[name] = (out[name] * factor).astype(out[name].dtype)
    return out
```

```python
from contextlib import ExitStack

import concourse.bass as bass
from concourse import mybir

F32 = mybir.dt.float32
F32R = mybir.dt.float32r
BF16 = mybir.dt.bfloat16
F16 = mybir.dt.float16
I32 = mybir.dt.int32
ALU = mybir.AluOpType
ACT = mybir.ActivationFunctionType
AX_X = mybir.AxisListType.X

P = 128
NEG_INF = -9000000000000000.0
LOWEST = -3.0e38
ALPHA = 0.2
EPS = 1e-5


def gat_resnorm_kernel(nc: bass.Bass, x: bass.AP, adj: bass.AP, w: bass.AP, a: bass.AP, out: bass.AP):
    B, N, D = x.shape
    H = a.shape[1]
    F = D // H
    TILES = N // P
    CHUNKS = D // P
    HALF = 512
    HALVES = D // HALF
    HH = H // HALVES
    BANKS = 4
    UNITS = 2 * TILES * HALVES
    SECOND = TILES * HALVES
    assert N == D and UNITS % BANKS == 0 and TILES == 8 and HALVES == 2

    with ExitStack() as ctx:
        def sb(name, shape, dt):
            return ctx.enter_context(nc.sbuf_tensor(name, shape, dt))

        def ps(name, shape, dt):
            return ctx.enter_context(nc.psum_tensor(name, shape, dt))

        def sem(name):
            return ctx.enter_context(nc.semaphore(name))

        w_hi = sb("w_hi", [P, CHUNKS, D], F32R)
        w_lo = sb("w_lo", [P, CHUNKS, D], F32R)
        wh_hi = sb("wh_hi", [P, TILES, D], F32R)
        wh_lo = sb("wh_lo", [P, TILES, D], F32R)
        adj_t = sb("adj_t", [P, TILES, N], F32R)
        xt_hi = sb("xt_hi", [P, 2, D], F32R)
        xt_lo = sb("xt_lo", [P, 2, D], F32R)
        x_in = sb("x_in", [P, 2, D], F32)
        adj_in = sb("adj_in", [P, N], I32)
        adj_h = sb("adj_h", [P, N], F16)
        work = sb("work", [P, 4, D], F32)
        h_new = work[:, 0, :]
        rows = work[:, 1:3, :]
        exps = work[:, 3, :]
        a_sum = sb("a_sum", [P, D], F32)
        scrap = sb("scrap", [P, D], BF16)
        count_scrap = sb("count_scrap", [P, N], BF16)
        ident = sb("ident", [P, P], F32)
        ident_h = sb("ident_h", [P, P], F16)
        score = sb("score", [P, TILES, H], F32)
        count = sb("count", [P, TILES], F32)
        absent = sb("absent", [P, TILES], F32)
        any_edge = sb("any_edge", [P, TILES], F32)
        all_edges = sb("all_edges", [P, TILES], F32)
        top = sb("top", [P, TILES, H], F32)
        below = sb("below", [P, 2, TILES, H], F32)
        weight = sb("weight", [P, 2, TILES, H], F32)
        total = sb("total", [P, TILES, H], F32)
        scale = sb("scale", [P, TILES, H], F32)
        row_sum = sb("row_sum", [P, 2], F32)
        neg_mean = sb("neg_mean", [P, 2], F32)
        sq_sum = sb("sq_sum", [P, 2], F32)
        variance = sb("variance", [P, 2], F32)
        rstd = sb("rstd", [P, 2], F32)
        shift = sb("shift", [P, 2], F32)
        per_feature = sb("per_feature", [P, 1], F32)
        eps = sb("eps", [P, 1], F32)
        minus_half = sb("minus_half", [P, 1], F32)

        acc = ps("acc", [P, BANKS, HALF], F32)
        xt_ps = ps("xt_ps", [P, CHUNKS, P], F32)
        adj_ps = ps("adj_ps", [P, TILES, P], F16)

        w_loaded = [sem(f"w_loaded{s}") for s in range(3)]
        w_split = sem("w_split")
        a_loaded = sem("a_loaded")
        a_summed = sem("a_summed")
        w_rounded = sem("w_rounded")
        zeroed = sem("zeroed")
        consts_ready = sem("consts_ready")
        x_loaded = [sem(f"x_loaded{s}") for s in range(2)]
        x_turned = sem("x_turned")
        xt_rounded = sem("xt_rounded")
        xt_split = sem("xt_split")
        adj_loaded = sem("adj_loaded")
        adj_cast = sem("adj_cast")
        adj_turned = sem("adj_turned")
        adj_t_ready = sem("adj_t_ready")
        adj_counted = sem("adj_counted")
        product_done = sem("product_done")
        bank_free = sem("bank_free")
        wh_rounded = sem("wh_rounded")
        wh_split = sem("wh_split")
        scored = sem("scored")
        exp_ready = sem("exp_ready")
        x_used = sem("x_used")
        relu_added = sem("relu_added")
        row_summed = sem("row_summed")
        mean_ready = sem("mean_ready")
        squares_ready = sem("squares_ready")
        below_ready = sem("below_ready")
        weight_ready = sem("weight_ready")
        dve_step = sem("dve_step")
        pool_step = sem("pool_step")
        act_step = sem("act_step")
        rstd_ready = sem("rstd_ready")
        normed = sem("normed")
        stored = [sem(f"stored{s}") for s in range(2)]

        x_rows = x.rearrange("b n d -> (b n) d")
        adj_rows = adj.rearrange("b n d -> (b n) d")
        out_rows = out.rearrange("b n d -> (b n) d")
        w_rows = w.rearrange("o k n -> (o k) n")
        a_row = a.rearrange("o h f l -> (o l) (h f)")

        block = ctx.enter_context(nc.Block())

        @block.sync
        def _(sp):
            def load_x(b, t, slot):
                sp.dma_start(x_in[:, slot, :], x_rows[bass.ds(b * N + t * P, P), :]).then_inc(x_loaded[slot], 16)

            def load_adj(b, t):
                sp.dma_start(adj_in[:, :], adj_rows[bass.ds(b * N + t * P, P), :])\
                  .then_inc(adj_loaded, 16)

            def load_w(c):
                sp.dma_start(work[:, c % 3, :], w_rows[c * P:(c + 1) * P, :]).then_inc(w_loaded[c % 3], 16)

            load_x(0, 0, 0)
            load_adj(0, 0)
            sp.dma_start(work[:, 1:3, :].rearrange("p t d -> p (t d)"),
                         a_row.to_broadcast([P, 2 * D])).then_inc(a_loaded, 16)
            load_w(0)
            sp.wait_ge(a_summed, 1)
            load_w(1)
            load_w(2)
            for c in range(3, CHUNKS):
                sp.wait_ge(w_split, c - 2)
                load_w(c)

            def graph(b, last):
                for t in range(TILES - 1):
                    if t == 1:
                        sp.wait_ge(x_used, 8 * b + 1)
                    else:
                        sp.wait_ge(x_turned, 8 * b + max(t, 1))
                    load_x(b, t + 1, t % 2)
                    sp.wait_ge(adj_cast, 8 * b + t + 1)
                    load_adj(b, t + 1)
                if not last:
                    sp.wait_ge(adj_cast, 8 * b + TILES)
                    load_adj(b + 1, 0)
                for i in range(TILES - 1):
                    if i < 2:
                        sp.wait_ge(x_turned, 8 * b + TILES - 1 + i)
                    else:
                        sp.wait_ge(x_used, 8 * b + i)
                    load_x(b, i, (i + 1) % 2)
                if not last:
                    sp.wait_ge(x_used, 8 * b + TILES - 1)
                    load_x(b + 1, 0, 0)
                sp.wait_ge(x_used, 8 * b + TILES)
                load_x(b, TILES - 1, 1)

            with sp.Fori(0, B - 1) as b:
                graph(b, False)
            graph(B - 1, True)

        @block.tensor
        def _(pe):
            def turn_x(g, slot, loads, first=False):
                pe.wait_ge(x_loaded[slot], 16 * loads)
                if not first:
                    pe.wait_ge(xt_split, g)
                for c in range(CHUNKS):
                    last = nc.tensor.transpose(xt_ps[:, c, :], x_in[:, slot, c * P:(c + 1) * P], ident[:, :])
                last.then_inc(x_turned, 1)

            def turn_adj(b, t):
                pe.wait_ge(adj_cast, 8 * b + t + 1)
                if t:
                    pe.wait_ge(adj_t_ready, 8 * b + t)
                for j in range(TILES):
                    last = nc.tensor.transpose(adj_ps[:, j, :], adj_h[:, j * P:(j + 1) * P], ident_h[:, :])
                last.then_inc(adj_turned, 1)

            def make_wh(b, t, h):
                if True:
                    u = t * HALVES + h
                    cols = slice(h * HALF, (h + 1) * HALF)
                    pe.wait_ge(bank_free, UNITS * b + u + 1)
                    pe.wait_ge(xt_split, 8 * b + t + 1)
                    for c in range(CHUNKS):
                        if u == 0:
                            pe.wait_ge(w_split, c + 1)
                        hi = xt_hi[:, t % 2, c * P:(c + 1) * P]
                        lo = xt_lo[:, t % 2, c * P:(c + 1) * P]
                        bank = acc[:, u % BANKS, :]
                        nc.tensor.matmul(bank, lo, w_hi[:, c, cols], start=(c == 0), stop=False)
                        nc.tensor.matmul(bank, hi, w_lo[:, c, cols], start=False, stop=False)
                        last = nc.tensor.matmul(bank, hi, w_hi[:, c, cols], start=False, stop=(c == CHUNKS - 1))
                    last.then_inc(product_done, 1)

            def gather(b, i):
                pe.wait_ge(adj_t_ready, 8 * b + i + 1)
                for h in range(HALVES):
                    u = SECOND + i * HALVES + h
                    cols = slice(h * HALF, (h + 1) * HALF)
                    pe.wait_ge(bank_free, UNITS * b + u + 1)
                    for j in range(TILES):
                        if i == 0:
                            pe.wait_ge(wh_split, SECOND * b + j * HALVES + h + 1)
                        edges = adj_t[:, i, j * P:(j + 1) * P]
                        bank = acc[:, u % BANKS, :]
                        nc.tensor.matmul(bank, edges, wh_lo[:, j, cols], start=(j == 0), stop=False)
                        last = nc.tensor.matmul(bank, edges, wh_hi[:, j, cols], start=False, stop=(j == TILES - 1))
                    last.then_inc(product_done, 1)

            def graph(b, last):
                for t in range(TILES):
                    make_wh(b, t, 0)
                    if t < TILES - 1:
                        turn_x(8 * b + t + 1, t % 2, 8 * b + t // 2 + (2 if t % 2 == 0 else 1))
                    turn_adj(b, t)
                    make_wh(b, t, 1)
                for i in range(TILES):
                    if i == TILES - 1 and not last:
                        turn_x(8 * b + TILES, 0, 8 * b + 9)
                    gather(b, i)

            pe.wait_ge(consts_ready, 2)
            turn_x(0, 0, 1, first=True)
            with pe.Fori(0, B - 1) as b:
                graph(b, False)
            graph(B - 1, True)

        @block.scalar
        def _(act):
            def cast_adj(g, first=False):
                act.wait_ge(adj_loaded, 16 * (g + 1))
                if not first:
                    act.wait_ge(adj_counted, g)
                nc.scalar.activation(adj_h[:, :], adj_in[:, :], ACT.Copy).then_inc(adj_cast, 1)

            def round_xt(g, slot):
                act.wait_ge(x_turned, g + 1)
                nc.scalar.activation(xt_hi[:, slot, :], xt_ps[:, :, :].rearrange("p c q -> p (c q)"), ACT.Copy)\
                    .then_inc(xt_rounded, 1)

            def round_wh(b, t, h):
                u = t * HALVES + h
                act.wait_ge(product_done, UNITS * b + u + 1)
                nc.scalar.activation(wh_hi[:, t, h * HALF:(h + 1) * HALF], acc[:, u % BANKS, :], ACT.Copy)\
                    .then_inc(wh_rounded, 1)

            def norm_squares(b, i):
                act.wait_ge(mean_ready, 8 * b + i + 1)
                nc.scalar.activation(scrap[:, :], rows[:, i % 2, :], ACT.Square, bias=neg_mean[:, i % 2:i % 2 + 1],
                                     accum_out=sq_sum[:, i % 2:i % 2 + 1]).then_inc(squares_ready, 1)

            def norm_store(b, i):
                s = i % 2
                act.wait_ge(rstd_ready, 8 * b + i + 1)
                nc.scalar.activation(rows[:, s, :], rows[:, s, :], ACT.Identity, bias=shift[:, s:s + 1],
                                     scale=rstd[:, s:s + 1]).then_inc(normed, 1)
                act.wait_ge(normed, 8 * b + i + 1)
                act.dma_start(out_rows[bass.ds(b * N + i * P, P), :], rows[:, s, :]).then_inc(stored[s], 16)

            def exp_neg_part(b, i, h):
                k = 16 * b + 2 * i + h
                part = exps[:, h * HALF:(h + 1) * HALF]
                act.wait_ge(bank_free, UNITS * b + SECOND + 2 * i + h + 1 + BANKS)
                nc.scalar.activation(part, h_new[:, h * HALF:(h + 1) * HALF], ACT.Relu, scale=-1.0)\
                    .then_inc(act_step, 1)
                act.wait_ge(act_step, k + 1)
                nc.scalar.activation(part, part, ACT.Exp, scale=-1.0).then_inc(exp_ready, 1)

            def graph(b, last):
                for t in range(TILES):
                    round_wh(b, t, 0)
                    if t < TILES - 1:
                        round_xt(8 * b + t + 1, (t + 1) % 2)
                    act.wait_ge(adj_turned, 8 * b + t + 1)
                    nc.scalar.activation(adj_t[:, t, :], adj_ps[:, :, :].rearrange("p j q -> p (j q)"), ACT.Copy)\
                        .then_inc(adj_t_ready, 1)
                    if t < TILES - 1 or not last:
                        cast_adj(8 * b + t + 1)
                    round_wh(b, t, 1)
                act.wait_ge(below_ready, b + 1)
                nc.scalar.activation(weight[:, :, :, :], below[:, :, :, :], ACT.Exp).then_inc(weight_ready, 1)
                for i in range(TILES):
                    if i == TILES - 1 and not last:
                        round_xt(8 * b + TILES, 0)
                    exp_neg_part(b, i, 0)
                    if i:
                        norm_store(b, i - 1)
                    exp_neg_part(b, i, 1)
                    norm_squares(b, i)
                norm_store(b, TILES - 1)

            cast_adj(0, first=True)
            round_xt(0, 0)
            for c in range(CHUNKS):
                act.wait_ge(w_loaded[c % 3], 16 * (c // 3 + 1))
                nc.scalar.activation(w_hi[:, c, :], work[:, c % 3, :], ACT.Copy).then_inc(w_rounded, 1)
            act.wait_ge(w_split, CHUNKS)
            with act.Fori(0, B - 1) as b:
                graph(b, False)
            graph(B - 1, True)
            for s in range(2):
                act.wait_ge(stored[s], 16 * (B * TILES // 2 + 1))

        @block.vector
        def _(dve):
            def split_xt(g, slot):
                dve.wait_ge(xt_rounded, g + 1)
                nc.vector.tensor_tensor(xt_lo[:, slot, :], xt_ps[:, :, :].rearrange("p c q -> p (c q)"),
                                        xt_hi[:, slot, :].bitcast(F32), ALU.subtract).then_inc(xt_split, 1)

            def count_edges(b, t):
                dve.wait_ge(adj_cast, 8 * b + t + 1)
                if t:
                    dve.wait_ge(adj_counted, 8 * b + t)
                nc.vector.tensor_scalar(count_scrap[:, :], adj_h[:, :], 0.0, None, ALU.not_equal, ALU.add,
                                        accum_out=count[:, t:t + 1]).then_inc(adj_counted, 1)

            def split_wh(b, t, h):
                u = t * HALVES + h
                cols = slice(h * HALF, (h + 1) * HALF)
                bank = acc[:, u % BANKS, :]
                dve.wait_ge(wh_rounded, SECOND * b + u + 1)
                nc.vector.tensor_tensor(wh_lo[:, t, cols], bank, wh_hi[:, t, cols].bitcast(F32), ALU.subtract)\
                    .then_inc(wh_split, 1)
                nc.vector.tensor_tensor(h_new[:, cols], bank, a_sum[:, cols], ALU.mult).then_inc(bank_free, 1)

            def score_wh(b, t, h):
                u = t * HALVES + h
                dve.wait_ge(bank_free, UNITS * b + u + 1 + BANKS)
                nc.vector.tensor_reduce(score[:, t, h * HH:(h + 1) * HH],
                                        h_new[:, h * HALF:(h + 1) * HALF].rearrange("p (h f) -> p h f", f=F),
                                        AX_X, ALU.add).then_inc(scored, 1)

            STEPS = 16

            def row_factors(b):
                done = [0]

                def step(ins):
                    done[0] += 1
                    ins.then_inc(dve_step, 1)
                    dve.wait_ge(dve_step, STEPS * b + done[0])

                def per_head(v):
                    return v[:, :].unsqueeze(2).to_broadcast([P, TILES, H])

                e_part, n_part = below[:, 0, :, :], below[:, 1, :, :]
                p, q = weight[:, 0, :, :], weight[:, 1, :, :]
                dve.wait_ge(scored, SECOND * (b + 1))
                dve.wait_ge(adj_counted, 8 * (b + 1))
                step(nc.vector.scalar_tensor_tensor(out=score[:, :, :], in0=score[:, :, :], scalar=ALPHA,
                                                    in1=score[:, :, :], op0=ALU.mult, op1=ALU.max))
                step(nc.vector.tensor_scalar(any_edge[:, :], count[:, :], 0.0, None, ALU.is_gt))
                step(nc.vector.tensor_scalar(all_edges[:, :], count[:, :], float(N), None, ALU.is_ge))
                step(nc.vector.tensor_scalar(absent[:, :], count[:, :], -1.0, float(N), ALU.mult, ALU.add))
                step(nc.vector.tensor_tensor(score[:, :, :], score[:, :, :], per_head(any_edge), ALU.mult))
                step(nc.vector.tensor_scalar(any_edge[:, :], any_edge[:, :], -NEG_INF, NEG_INF, ALU.mult, ALU.add))
                step(nc.vector.tensor_tensor(score[:, :, :], score[:, :, :], per_head(any_edge), ALU.add))
                step(nc.vector.tensor_scalar(all_edges[:, :], all_edges[:, :], LOWEST, NEG_INF, ALU.mult, ALU.add))
                step(nc.vector.tensor_tensor(top[:, :, :], score[:, :, :], per_head(all_edges), ALU.max))
                step(nc.vector.tensor_tensor(e_part, score[:, :, :], top[:, :, :], ALU.subtract))
                step(nc.vector.tensor_scalar(n_part, top[:, :, :], -1.0, NEG_INF, ALU.mult, ALU.add))
                nc.vector.tensor_scalar(n_part, n_part, 0.0, None, ALU.min).then_inc(below_ready, 1)
                dve.wait_ge(weight_ready, b + 1)
                step(nc.vector.tensor_tensor(total[:, :, :], p, per_head(count), ALU.mult))
                step(nc.vector.tensor_tensor(q, q, per_head(absent), ALU.mult))
                step(nc.vector.tensor_tensor(total[:, :, :], total[:, :, :], q, ALU.add))
                step(nc.vector.reciprocal(total[:, :, :], total[:, :, :]))
                nc.vector.tensor_tensor(scale[:, :, :], p, total[:, :, :], ALU.mult).then_inc(dve_step, 1)
                dve.wait_ge(dve_step, STEPS * b + done[0] + 1)
                assert done[0] + 1 == STEPS

            nc.vector.memset(neg_mean[:, :], 0.0).then_inc(x_used, 1)
            nc.vector.memset(per_feature[:, :], 1.0 / D).then_inc(stored[0], 16)
            nc.vector.memset(eps[:, :], EPS).then_inc(stored[1], 16)
            nc.vector.memset(minus_half[:, :], -0.5).then_inc(bank_free, BANKS)
            dve.wait_ge(a_loaded, 16)
            pair = work[:, 1:3, :].rearrange("p t (h s f) -> p (t h) s f", s=2, f=F)
            nc.vector.tensor_tensor(a_sum[:, :].rearrange("p (h f) -> p h f", f=F), pair[:, :, 0, :],
                                    pair[:, :, 1, :], ALU.add).then_inc(a_summed, 1)
            split_xt(0, 0)
            for c in range(CHUNKS):
                dve.wait_ge(w_rounded, c + 1)
                nc.vector.tensor_tensor(w_lo[:, c, :], work[:, c % 3, :], w_hi[:, c, :].bitcast(F32),
                                        ALU.subtract).then_inc(w_split, 1)
            dve.wait_ge(w_split, CHUNKS)

            def graph(b, last):
                for t in range(TILES):
                    split_wh(b, t, 0)
                    score_wh(b, t, 0)
                    if t < TILES - 1:
                        split_xt(8 * b + t + 1, (t + 1) % 2)
                    count_edges(b, t)
                    split_wh(b, t, 1)
                    score_wh(b, t, 1)
                row_factors(b)
                for i in range(TILES):
                    s = i % 2
                    if i == TILES - 1 and not last:
                        split_xt(8 * b + TILES, 0)
                    for h in range(HALVES):
                        u = SECOND + i * HALVES + h
                        dve.wait_ge(product_done, UNITS * b + u + 1)
                        nc.vector.tensor_tensor(
                            h_new[:, h * HALF:(h + 1) * HALF].rearrange("p (h f) -> p h f", f=F),
                            acc[:, u % BANKS, :].rearrange("p (h f) -> p h f", f=F),
                            scale[:, i, h * HH:(h + 1) * HH].unsqueeze(2).to_broadcast([P, HH, F]),
                            ALU.mult).then_inc(bank_free, 1)
                    n = TILES - 1 + i if i < TILES - 1 else 2 * TILES - 1
                    slot = n % 2
                    loads = 8 * b + n // 2 + (2 if n % 2 == 0 else 1)
                    dve.wait_ge(bank_free, UNITS * b + SECOND + 2 * i + 2 + BANKS)
                    dve.wait_ge(x_loaded[slot], 16 * loads)
                    nc.vector.scalar_tensor_tensor(out=x_in[:, slot, :], in0=h_new, scalar=0.0,
                                                   in1=x_in[:, slot, :], op0=ALU.max, op1=ALU.add)\
                        .then_inc(relu_added, 1)
                    dve.wait_ge(relu_added, 8 * b + i + 1)
                    dve.wait_ge(exp_ready, 16 * b + 2 * i + 2)
                    dve.wait_ge(stored[s], 64 * b + 16 * (i // 2) + 16)
                    nc.vector.scalar_tensor_tensor(out=rows[:, s, :], in0=exps, scalar=-1.0,
                                                   in1=x_in[:, slot, :], op0=ALU.add, op1=ALU.add,
                                                   accum_out=row_sum[:, s:s + 1]).then_inc(x_used, 1)
                    dve.wait_ge(x_used, 8 * b + i + 2)
                    nc.vector.tensor_scalar(neg_mean[:, s:s + 1], row_sum[:, s:s + 1], -1.0 / D, None, ALU.mult)\
                        .then_inc(mean_ready, 1)

            with dve.Fori(0, B - 1) as b:
                graph(b, False)
            graph(B - 1, True)

        @block.gpsimd
        def _(pool):
            nc.gpsimd.memset(ident[:, :], 0.0).then_inc(zeroed, 1)
            nc.gpsimd.memset(ident_h[:, :], 0.0).then_inc(zeroed, 1)
            pool.wait_ge(zeroed, 2)
            for m in (ident, ident_h):
                nc.gpsimd.affine_select(out=m[:, :], in_=m[:, :], compare_op=ALU.not_equal, fill=1.0,
                                        base=0, pattern=[[-1, P]], channel_multiplier=1).then_inc(consts_ready, 1)
            pool.wait_ge(bank_free, BANKS)

            def tile(g, s):
                one = slice(s, s + 1)
                pool.wait_ge(squares_ready, g + 1)
                nc.gpsimd.tensor_tensor(variance[:, one], sq_sum[:, one], per_feature[:, :], ALU.mult)\
                    .then_inc(pool_step, 1)
                pool.wait_ge(pool_step, 3 * g + 1)
                nc.gpsimd.tensor_tensor(variance[:, one], variance[:, one], eps[:, :], ALU.add)\
                    .then_inc(pool_step, 1)
                pool.wait_ge(pool_step, 3 * g + 2)
                nc.gpsimd.tensor_tensor(rstd[:, one], variance[:, one], minus_half[:, :], ALU.pow)\
                    .then_inc(pool_step, 1)
                pool.wait_ge(pool_step, 3 * g + 3)
                nc.gpsimd.tensor_tensor(shift[:, one], neg_mean[:, one], rstd[:, one], ALU.mult)\
                    .then_inc(rstd_ready, 1)

            with pool.Fori(0, B * TILES, 2) as g:
                tile(g, 0)
                tile(g + 1, 1)


def kernel(x, adj, L0_gnn_W, L0_gnn_a):
    import numpy as _np
    import concourse.bacc as _bacc
    from concourse import mybir as _mybir
    from concourse.bass_utils import run_bass_kernel_spmd as _run

    nc = _bacc.Bacc("TRN2", target_bir_lowering=False, num_devices=1, dynamic_dma_scratch_size=4096)
    arrays, args = {}, []
    for name, value in (("x", x), ("adj", adj), ("W", L0_gnn_W), ("a", L0_gnn_a)):
        v = _np.ascontiguousarray(value)
        arrays[f"in_{name}"] = v
        args.append(nc.dram_tensor(f"in_{name}", v.shape, _mybir.dt.from_np(v.dtype), kind="ExternalInput").ap())
    args.append(nc.dram_tensor("out", arrays["in_x"].shape, _mybir.dt.float32, kind="ExternalOutput").ap())
    gat_resnorm_kernel(nc, *args)
    r = _run(nc, [arrays], core_ids=[0])
    return r.results[0]["out"]
```

```python
from contextlib import ExitStack

import concourse.bass as bass
from concourse import mybir

F32 = mybir.dt.float32
F32R = mybir.dt.float32r
BF16 = mybir.dt.bfloat16
F16 = mybir.dt.float16
I32 = mybir.dt.int32
ALU = mybir.AluOpType
ACT = mybir.ActivationFunctionType
AX_X = mybir.AxisListType.X

P = 128
NEG_INF = -9000000000000000.0
LOWEST = -3.0e38
ALPHA = 0.2
EPS = 1e-5


def gat_resnorm_kernel(nc: bass.Bass, x: bass.AP, adj: bass.AP, w: bass.AP, a: bass.AP, out: bass.AP):
    B, N, D = x.shape
    H = a.shape[1]
    F = D // H
    TILES = N // P
    CHUNKS = D // P
    HALF = 512
    HALVES = D // HALF
    HH = H // HALVES
    BANKS = 4
    UNITS = 2 * TILES * HALVES
    SECOND = TILES * HALVES
    assert N == D and UNITS % BANKS == 0 and TILES == 8 and HALVES == 2

    with ExitStack() as ctx:
        def sb(name, shape, dt):
            return ctx.enter_context(nc.sbuf_tensor(name, shape, dt))

        def ps(name, shape, dt):
            return ctx.enter_context(nc.psum_tensor(name, shape, dt))

        def sem(name):
            return ctx.enter_context(nc.semaphore(name))

        w_hi = sb("w_hi", [P, CHUNKS, D], F32R)
        w_lo = sb("w_lo", [P, CHUNKS, D], F32R)
        wh_hi = sb("wh_hi", [P, TILES, D], F32R)
        wh_lo = sb("wh_lo", [P, TILES, D], F32R)
        adj_t = sb("adj_t", [P, TILES, N], F32R)
        xt_hi = sb("xt_hi", [P, 2, D], F32R)
        xt_lo = sb("xt_lo", [P, 2, D], F32R)
        x_in = sb("x_in", [P, 2, D], F32)
        adj_in = sb("adj_in", [P, N], I32)
        adj_h = sb("adj_h", [P, N], F16)
        adj_x = sb("adj_x", [P, TILES, P], F16)
        work = sb("work", [P, 4, D], F32)
        h_new = work[:, 0, :]
        rows = work[:, 1:3, :]
        exps = work[:, 3, :]
        a_sum = sb("a_sum", [P, D], F32)
        scrap = sb("scrap", [P, D], BF16)
        ident = sb("ident", [P, P], F32)
        score = sb("score", [P, TILES, H], F32)
        count = sb("count", [P, TILES], F32)
        absent = sb("absent", [P, TILES], F32)
        any_edge = sb("any_edge", [P, TILES], F32)
        all_edges = sb("all_edges", [P, TILES], F32)
        top = sb("top", [P, TILES, H], F32)
        below = sb("below", [P, 2, TILES, H], F32)
        weight = sb("weight", [P, 2, TILES, H], F32)
        total = sb("total", [P, TILES, H], F32)
        scale = sb("scale", [P, TILES, H], F32)
        row_sum = sb("row_sum", [P, 2], F32)
        neg_mean = sb("neg_mean", [P, 2], F32)
        sq_sum = sb("sq_sum", [P, 2], F32)
        variance = sb("variance", [P, 2], F32)
        rstd = sb("rstd", [P, 2], F32)
        shift = sb("shift", [P, 2], F32)
        per_feature = sb("per_feature", [P, 1], F32)
        eps = sb("eps", [P, 1], F32)
        minus_half = sb("minus_half", [P, 1], F32)

        acc = ps("acc", [P, BANKS, HALF], F32)
        xt_ps = ps("xt_ps", [P, CHUNKS, P], F32)

        w_loaded = [sem(f"w_loaded{s}") for s in range(4)]
        w_split = sem("w_split")
        a_loaded = sem("a_loaded")
        a_summed = sem("a_summed")
        w_rounded = sem("w_rounded")
        zeroed = sem("zeroed")
        consts_ready = sem("consts_ready")
        x_loaded = [sem(f"x_loaded{s}") for s in range(2)]
        x_turned = sem("x_turned")
        xt_rounded = sem("xt_rounded")
        xt_split = sem("xt_split")
        adj_loaded = sem("adj_loaded")
        adj_cast = sem("adj_cast")
        adj_turned = sem("adj_turned")
        adj_t_ready = sem("adj_t_ready")
        adj_counted = sem("adj_counted")
        product_done = sem("product_done")
        bank_free = sem("bank_free")
        wh_rounded = sem("wh_rounded")
        wh_split = sem("wh_split")
        scored = sem("scored")
        exp_ready = sem("exp_ready")
        x_used = sem("x_used")
        row_summed = sem("row_summed")
        mean_ready = sem("mean_ready")
        squares_ready = sem("squares_ready")
        below_ready = sem("below_ready")
        weight_ready = sem("weight_ready")
        dve_step = sem("dve_step")
        pool_step = sem("pool_step")
        act_step = sem("act_step")
        rstd_ready = sem("rstd_ready")
        normed = sem("normed")
        stored = [sem(f"stored{s}") for s in range(2)]

        x_rows = x.rearrange("b n d -> (b n) d")
        adj_rows = adj.rearrange("b n d -> (b n) d")
        out_rows = out.rearrange("b n d -> (b n) d")
        w_rows = w.rearrange("o k n -> (o k) n")
        a_row = a.rearrange("o h f l -> (o l) (h f)")

        block = ctx.enter_context(nc.Block())

        @block.sync
        def _(sp):
            def load_x(b, t, slot):
                sp.dma_start(x_in[:, slot, :], x_rows[bass.ds(b * N + t * P, P), :]).then_inc(x_loaded[slot], 16)

            def load_adj(b, t):
                sp.dma_start(adj_in[:, :], adj_rows[bass.ds(b * N + t * P, P), :])\
                  .then_inc(adj_loaded, 16)

            def load_w(c):
                sp.dma_start(work[:, c % 4, :], w_rows[c * P:(c + 1) * P, :]).then_inc(w_loaded[c % 4], 16)

            def wait_turn_adj(b, t):
                sp.wait_ge(adj_cast, 8 * b + t + 1)
                if t:
                    sp.wait_ge(adj_t_ready, 8 * b + t)

            def turn_adj():
                sp.dma_start_transpose(adj_x[:, :, :], adj_h[:, :]).then_inc(adj_turned, 16)

            load_x(0, 0, 0)
            for c in range(4):
                load_w(c)
            for c in range(4, CHUNKS):
                sp.wait_ge(w_split, c - 3)
                load_w(c)
            load_adj(0, 0)

            def graph(b, last):
                for t in range(TILES - 1):
                    if t == 1:
                        sp.wait_ge(x_used, 8 * b + 1)
                    else:
                        sp.wait_ge(x_turned, 8 * b + max(t, 1))
                    load_x(b, t + 1, t % 2)
                    wait_turn_adj(b, t)
                    load_adj(b, t + 1)
                    turn_adj()
                wait_turn_adj(b, TILES - 1)
                if not last:
                    load_adj(b + 1, 0)
                    turn_adj()
                for i in range(TILES - 1):
                    if i < 2:
                        sp.wait_ge(x_turned, 8 * b + TILES - 1 + i)
                    else:
                        sp.wait_ge(x_used, 8 * b + i)
                    load_x(b, i, (i + 1) % 2)
                    if i == 0 and last:
                        turn_adj()
                if not last:
                    sp.wait_ge(x_used, 8 * b + TILES - 1)
                    load_x(b + 1, 0, 0)
                sp.wait_ge(x_used, 8 * b + TILES)
                load_x(b, TILES - 1, 1)

            with sp.Fori(0, B - 1) as b:
                graph(b, False)
            graph(B - 1, True)

        @block.tensor
        def _(pe):
            def turn_x(g, slot, loads, first=False):
                pe.wait_ge(x_loaded[slot], 16 * loads)
                if not first:
                    pe.wait_ge(xt_split, g)
                for c in range(CHUNKS):
                    last = nc.tensor.transpose(xt_ps[:, c, :], x_in[:, slot, c * P:(c + 1) * P], ident[:, :])
                last.then_inc(x_turned, 1)

            def make_wh(b, t, h):
                if True:
                    u = t * HALVES + h
                    cols = slice(h * HALF, (h + 1) * HALF)
                    pe.wait_ge(bank_free, UNITS * b + u + 1)
                    pe.wait_ge(xt_split, 8 * b + t + 1)
                    for c in range(CHUNKS):
                        if u == 0:
                            pe.wait_ge(w_split, c + 1)
                        hi = xt_hi[:, t % 2, c * P:(c + 1) * P]
                        lo = xt_lo[:, t % 2, c * P:(c + 1) * P]
                        bank = acc[:, u % BANKS, :]
                        nc.tensor.matmul(bank, lo, w_hi[:, c, cols], start=(c == 0), stop=False)
                        nc.tensor.matmul(bank, hi, w_lo[:, c, cols], start=False, stop=False)
                        last = nc.tensor.matmul(bank, hi, w_hi[:, c, cols], start=False, stop=(c == CHUNKS - 1))
                    last.then_inc(product_done, 1)

            def gather(b, i, halves):
                pe.wait_ge(adj_t_ready, 8 * b + i + 1)
                for h in halves:
                    u = SECOND + i * HALVES + h
                    cols = slice(h * HALF, (h + 1) * HALF)
                    pe.wait_ge(bank_free, UNITS * b + u + 1)
                    for j in range(TILES):
                        if i == 0:
                            pe.wait_ge(wh_split, SECOND * b + j * HALVES + h + 1)
                        edges = adj_t[:, i, j * P:(j + 1) * P]
                        bank = acc[:, u % BANKS, :]
                        nc.tensor.matmul(bank, edges, wh_lo[:, j, cols], start=(j == 0), stop=False)
                        last = nc.tensor.matmul(bank, edges, wh_hi[:, j, cols], start=False, stop=(j == TILES - 1))
                    last.then_inc(product_done, 1)

            def graph(b, last):
                for t in range(TILES):
                    make_wh(b, t, 0)
                    if t < TILES - 1:
                        turn_x(8 * b + t + 1, t % 2, 8 * b + t // 2 + (2 if t % 2 == 0 else 1))
                    make_wh(b, t, 1)
                for i in range(TILES):
                    gather(b, i, [0])
                    if i == TILES - 1 and not last:
                        turn_x(8 * b + TILES, 0, 8 * b + 9)
                    gather(b, i, [1])

            pe.wait_ge(consts_ready, 1)
            turn_x(0, 0, 1, first=True)
            with pe.Fori(0, B - 1) as b:
                graph(b, False)
            graph(B - 1, True)

        @block.scalar
        def _(act):
            def cast_adj(g, first=False):
                act.wait_ge(adj_loaded, 16 * (g + 1))
                if not first:
                    act.wait_ge(adj_counted, g)
                nc.scalar.activation(adj_h[:, :], adj_in[:, :], ACT.Copy).then_inc(adj_cast, 1)

            def round_xt(g, slot):
                act.wait_ge(x_turned, g + 1)
                nc.scalar.activation(xt_hi[:, slot, :], xt_ps[:, :, :].rearrange("p c q -> p (c q)"), ACT.Copy)\
                    .then_inc(xt_rounded, 1)

            def round_wh(b, t, h):
                u = t * HALVES + h
                act.wait_ge(product_done, UNITS * b + u + 1)
                nc.scalar.activation(wh_hi[:, t, h * HALF:(h + 1) * HALF], acc[:, u % BANKS, :], ACT.Copy)\
                    .then_inc(wh_rounded, 1)

            def norm_squares(b, i):
                act.wait_ge(mean_ready, 8 * b + i + 1)
                nc.scalar.activation(scrap[:, :], rows[:, i % 2, :], ACT.Square, bias=neg_mean[:, i % 2:i % 2 + 1],
                                     accum_out=sq_sum[:, i % 2:i % 2 + 1]).then_inc(squares_ready, 1)

            def norm_store(b, i):
                s = i % 2
                act.wait_ge(rstd_ready, 8 * b + i + 1)
                nc.scalar.activation(rows[:, s, :], rows[:, s, :], ACT.Identity, bias=shift[:, s:s + 1],
                                     scale=rstd[:, s:s + 1]).then_inc(normed, 1)
                act.wait_ge(normed, 8 * b + i + 1)
                act.dma_start(out_rows[bass.ds(b * N + i * P, P), :], rows[:, s, :]).then_inc(stored[s], 16)

            def exp_neg_part(b, i, h):
                k = 16 * b + 2 * i + h
                part = exps[:, h * HALF:(h + 1) * HALF]
                act.wait_ge(bank_free, UNITS * b + SECOND + 2 * i + h + 1 + BANKS)
                nc.scalar.activation(part, h_new[:, h * HALF:(h + 1) * HALF], ACT.Relu, scale=-1.0)\
                    .then_inc(act_step, 1)
                act.wait_ge(act_step, k + 1)
                nc.scalar.activation(part, part, ACT.Exp, scale=-1.0).then_inc(exp_ready, 1)

            def graph(b, first, last):
                for t in range(TILES):
                    round_wh(b, t, 0)
                    if t < TILES - 1:
                        round_xt(8 * b + t + 1, (t + 1) % 2)
                    if t == 0 and not first:
                        norm_store(b - 1, TILES - 1)
                    act.wait_ge(adj_turned, 16 * (8 * b + t + 1))
                    nc.scalar.activation(adj_t[:, t, :], adj_x[:, :, :].rearrange("p j q -> p (j q)"), ACT.Copy)\
                        .then_inc(adj_t_ready, 1)
                    if t < TILES - 1 or not last:
                        cast_adj(8 * b + t + 1)
                    round_wh(b, t, 1)
                act.wait_ge(below_ready, b + 1)
                nc.scalar.activation(weight[:, :, :, :], below[:, :, :, :], ACT.Exp).then_inc(weight_ready, 1)
                for i in range(TILES):
                    if i == TILES - 1 and not last:
                        round_xt(8 * b + TILES, 0)
                    exp_neg_part(b, i, 0)
                    exp_neg_part(b, i, 1)
                    if i:
                        norm_store(b, i - 1)
                    norm_squares(b, i)
            round_xt(0, 0)
            for c in range(CHUNKS):
                act.wait_ge(w_loaded[c % 4], 16 * (c // 4 + 1))
                nc.scalar.activation(w_hi[:, c, :], work[:, c % 4, :], ACT.Copy).then_inc(w_rounded, 1)
            act.wait_ge(w_split, CHUNKS - 1)
            act.dma_start(work[:, 1:3, :].rearrange("p t d -> p (t d)"),
                         a_row.to_broadcast([P, 2 * D])).then_inc(a_loaded, 16)
            cast_adj(0, first=True)
            act.wait_ge(a_summed, 1)
            graph(0, True, False)
            with act.Fori(1, B - 1) as b:
                graph(b, False, False)
            graph(B - 1, False, True)
            norm_store(B - 1, TILES - 1)
            for s in range(2):
                act.wait_ge(stored[s], 16 * B * TILES // 2)

        @block.vector
        def _(dve):
            def split_xt(g, slot):
                dve.wait_ge(xt_rounded, g + 1)
                nc.vector.tensor_tensor(xt_lo[:, slot, :], xt_ps[:, :, :].rearrange("p c q -> p (c q)"),
                                        xt_hi[:, slot, :].bitcast(F32), ALU.subtract).then_inc(xt_split, 1)

            def count_edges(b, t):
                dve.wait_ge(adj_cast, 8 * b + t + 1)
                if t:
                    dve.wait_ge(adj_counted, 8 * b + t)
                nc.vector.tensor_scalar(exps, adj_h[:, :], 0.0, None, ALU.not_equal, ALU.add,
                                        accum_out=count[:, t:t + 1]).then_inc(adj_counted, 1)

            def split_wh(b, t, h):
                u = t * HALVES + h
                cols = slice(h * HALF, (h + 1) * HALF)
                bank = acc[:, u % BANKS, :]
                dve.wait_ge(wh_rounded, SECOND * b + u + 1)
                nc.vector.tensor_tensor(wh_lo[:, t, cols], bank, wh_hi[:, t, cols].bitcast(F32), ALU.subtract)\
                    .then_inc(wh_split, 1)
                nc.vector.tensor_tensor(h_new[:, cols], bank, a_sum[:, cols], ALU.mult).then_inc(bank_free, 1)

            def score_wh(b, t, h):
                u = t * HALVES + h
                dve.wait_ge(bank_free, UNITS * b + u + 1 + BANKS)
                nc.vector.tensor_reduce(score[:, t, h * HH:(h + 1) * HH],
                                        h_new[:, h * HALF:(h + 1) * HALF].rearrange("p (h f) -> p h f", f=F),
                                        AX_X, ALU.add).then_inc(scored, 1)

            STEPS = 16

            def row_factors(b):
                done = [0]

                def step(ins):
                    done[0] += 1
                    ins.then_inc(dve_step, 1)
                    dve.wait_ge(dve_step, STEPS * b + done[0])

                def per_head(v):
                    return v[:, :].unsqueeze(2).to_broadcast([P, TILES, H])

                e_part, n_part = below[:, 0, :, :], below[:, 1, :, :]
                p, q = weight[:, 0, :, :], weight[:, 1, :, :]
                dve.wait_ge(scored, SECOND * (b + 1))
                dve.wait_ge(adj_counted, 8 * (b + 1))
                step(nc.vector.scalar_tensor_tensor(out=score[:, :, :], in0=score[:, :, :], scalar=ALPHA,
                                                    in1=score[:, :, :], op0=ALU.mult, op1=ALU.max))
                step(nc.vector.tensor_scalar(any_edge[:, :], count[:, :], 0.0, None, ALU.is_gt))
                step(nc.vector.tensor_scalar(all_edges[:, :], count[:, :], float(N), None, ALU.is_ge))
                step(nc.vector.tensor_scalar(absent[:, :], count[:, :], -1.0, float(N), ALU.mult, ALU.add))
                step(nc.vector.tensor_tensor(score[:, :, :], score[:, :, :], per_head(any_edge), ALU.mult))
                step(nc.vector.tensor_scalar(any_edge[:, :], any_edge[:, :], -NEG_INF, NEG_INF, ALU.mult, ALU.add))
                step(nc.vector.tensor_tensor(score[:, :, :], score[:, :, :], per_head(any_edge), ALU.add))
                step(nc.vector.tensor_scalar(all_edges[:, :], all_edges[:, :], LOWEST, NEG_INF, ALU.mult, ALU.add))
                step(nc.vector.tensor_tensor(top[:, :, :], score[:, :, :], per_head(all_edges), ALU.max))
                step(nc.vector.tensor_tensor(e_part, score[:, :, :], top[:, :, :], ALU.subtract))
                step(nc.vector.tensor_scalar(n_part, top[:, :, :], -1.0, NEG_INF, ALU.mult, ALU.add))
                nc.vector.tensor_scalar(n_part, n_part, 0.0, None, ALU.min).then_inc(below_ready, 1)
                dve.wait_ge(weight_ready, b + 1)
                step(nc.vector.tensor_tensor(total[:, :, :], p, per_head(count), ALU.mult))
                step(nc.vector.tensor_tensor(q, q, per_head(absent), ALU.mult))
                step(nc.vector.tensor_tensor(total[:, :, :], total[:, :, :], q, ALU.add))
                step(nc.vector.reciprocal(total[:, :, :], total[:, :, :]))
                nc.vector.tensor_tensor(scale[:, :, :], p, total[:, :, :], ALU.mult).then_inc(dve_step, 1)
                dve.wait_ge(dve_step, STEPS * b + done[0] + 1)
                assert done[0] + 1 == STEPS

            nc.vector.memset(neg_mean[:, :], 0.0).then_inc(x_used, 1)
            nc.vector.memset(per_feature[:, :], 1.0 / D)
            nc.vector.memset(eps[:, :], EPS)
            nc.vector.memset(minus_half[:, :], -0.5).then_inc(bank_free, BANKS)
            split_xt(0, 0)
            for c in range(CHUNKS):
                dve.wait_ge(w_rounded, c + 1)
                nc.vector.tensor_tensor(w_lo[:, c, :], work[:, c % 4, :], w_hi[:, c, :].bitcast(F32),
                                        ALU.subtract).then_inc(w_split, 1)
            dve.wait_ge(a_loaded, 16)
            pair = work[:, 1:3, :].rearrange("p t (h s f) -> p (t h) s f", s=2, f=F)
            nc.vector.tensor_tensor(a_sum[:, :].rearrange("p (h f) -> p h f", f=F), pair[:, :, 0, :],
                                    pair[:, :, 1, :], ALU.add).then_inc(a_summed, 1)
            dve.wait_ge(a_summed, 1)

            def graph(b, first, last):
                for t in range(TILES):
                    split_wh(b, t, 0)
                    score_wh(b, t, 0)
                    if t < TILES - 1:
                        split_xt(8 * b + t + 1, (t + 1) % 2)
                    count_edges(b, t)
                    split_wh(b, t, 1)
                    score_wh(b, t, 1)
                row_factors(b)
                for i in range(TILES):
                    s = i % 2
                    for h in range(HALVES):
                        if h == 1 and i == TILES - 1 and not last:
                            split_xt(8 * b + TILES, 0)
                        u = SECOND + i * HALVES + h
                        dve.wait_ge(product_done, UNITS * b + u + 1)
                        nc.vector.tensor_tensor(
                            h_new[:, h * HALF:(h + 1) * HALF].rearrange("p (h f) -> p h f", f=F),
                            acc[:, u % BANKS, :].rearrange("p (h f) -> p h f", f=F),
                            scale[:, i, h * HH:(h + 1) * HH].unsqueeze(2).to_broadcast([P, HH, F]),
                            ALU.mult).then_inc(bank_free, 1)
                    n = TILES - 1 + i if i < TILES - 1 else 2 * TILES - 1
                    slot = n % 2
                    loads = 8 * b + n // 2 + (2 if n % 2 == 0 else 1)
                    dve.wait_ge(bank_free, UNITS * b + SECOND + 2 * i + 2 + BANKS)
                    dve.wait_ge(x_loaded[slot], 16 * loads)
                    if not first or i >= 2:
                        dve.wait_ge(stored[s], 64 * b + 16 * (i // 2))
                    nc.vector.scalar_tensor_tensor(out=rows[:, s, :], in0=h_new, scalar=0.0,
                                                   in1=x_in[:, slot, :], op0=ALU.max, op1=ALU.add)\
                        .then_inc(x_used, 1)
                    dve.wait_ge(x_used, 8 * b + i + 2)
                    dve.wait_ge(exp_ready, 16 * b + 2 * i + 2)
                    nc.vector.scalar_tensor_tensor(out=rows[:, s, :], in0=exps, scalar=-1.0,
                                                   in1=rows[:, s, :], op0=ALU.add, op1=ALU.add,
                                                   accum_out=row_sum[:, s:s + 1]).then_inc(row_summed, 1)
                    dve.wait_ge(row_summed, 8 * b + i + 1)
                    nc.vector.tensor_scalar(neg_mean[:, s:s + 1], row_sum[:, s:s + 1], -1.0 / D, None, ALU.mult)\
                        .then_inc(mean_ready, 1)

            graph(0, True, False)
            with dve.Fori(1, B - 1) as b:
                graph(b, False, False)
            graph(B - 1, False, True)

        @block.gpsimd
        def _(pool):
            nc.gpsimd.memset(ident[:, :], 0.0).then_inc(zeroed, 1)
            pool.wait_ge(zeroed, 1)
            nc.gpsimd.affine_select(out=ident[:, :], in_=ident[:, :], compare_op=ALU.not_equal, fill=1.0,
                                    base=0, pattern=[[-1, P]], channel_multiplier=1).then_inc(consts_ready, 1)
            pool.wait_ge(bank_free, BANKS)

            def tile(g, s):
                one = slice(s, s + 1)
                pool.wait_ge(squares_ready, g + 1)
                nc.gpsimd.tensor_tensor(variance[:, one], sq_sum[:, one], per_feature[:, :], ALU.mult)\
                    .then_inc(pool_step, 1)
                pool.wait_ge(pool_step, 3 * g + 1)
                nc.gpsimd.tensor_tensor(variance[:, one], variance[:, one], eps[:, :], ALU.add)\
                    .then_inc(pool_step, 1)
                pool.wait_ge(pool_step, 3 * g + 2)
                nc.gpsimd.tensor_tensor(rstd[:, one], variance[:, one], minus_half[:, :], ALU.pow)\
                    .then_inc(pool_step, 1)
                pool.wait_ge(pool_step, 3 * g + 3)
                nc.gpsimd.tensor_tensor(shift[:, one], neg_mean[:, one], rstd[:, one], ALU.mult)\
                    .then_inc(rstd_ready, 1)

            with pool.Fori(0, B * TILES, 2) as g:
                tile(g, 0)
                tile(g + 1, 1)


def kernel(x, adj, L0_gnn_W, L0_gnn_a):
    import numpy as _np
    import concourse.bacc as _bacc
    from concourse import mybir as _mybir
    from concourse.bass_utils import run_bass_kernel_spmd as _run

    nc = _bacc.Bacc("TRN2", target_bir_lowering=False, num_devices=1, dynamic_dma_scratch_size=4096)
    arrays, args = {}, []
    for name, value in (("x", x), ("adj", adj), ("W", L0_gnn_W), ("a", L0_gnn_a)):
        v = _np.ascontiguousarray(value)
        arrays[f"in_{name}"] = v
        args.append(nc.dram_tensor(f"in_{name}", v.shape, _mybir.dt.from_np(v.dtype), kind="ExternalInput").ap())
    args.append(nc.dram_tensor("out", arrays["in_x"].shape, _mybir.dt.float32, kind="ExternalOutput").ap())
    gat_resnorm_kernel(nc, *args)
    r = _run(nc, [arrays], core_ids=[0])
    return r.results[0]["out"]
```

```python
from contextlib import ExitStack

import concourse.bass as bass
from concourse import mybir

F32 = mybir.dt.float32
F32R = mybir.dt.float32r
BF16 = mybir.dt.bfloat16
F16 = mybir.dt.float16
I32 = mybir.dt.int32
U16 = mybir.dt.uint16
ALU = mybir.AluOpType
ACT = mybir.ActivationFunctionType
AX_X = mybir.AxisListType.X

P = 128
NEG_INF = -9000000000000000.0
LOWEST = -3.0e38
ALPHA = 0.2
EPS = 1e-5


def gat_resnorm_kernel(nc: bass.Bass, x: bass.AP, adj: bass.AP, w: bass.AP, a: bass.AP, out: bass.AP):
    B, N, D = x.shape
    H = a.shape[1]
    F = D // H
    TILES = N // P
    CHUNKS = D // P
    HALF = 512
    HALVES = D // HALF
    HH = H // HALVES
    BANKS = 4
    UNITS = 2 * TILES * HALVES
    SECOND = TILES * HALVES
    BY_PE = 2
    BY_DMA = TILES - BY_PE
    STORES = 16 * TILES // 2
    assert N == D and UNITS % BANKS == 0 and TILES == 8 and HALVES == 2

    with ExitStack() as ctx:
        def sb(name, shape, dt):
            return ctx.enter_context(nc.sbuf_tensor(name, shape, dt))

        def ps(name, shape, dt):
            return ctx.enter_context(nc.psum_tensor(name, shape, dt))

        def sem(name):
            return ctx.enter_context(nc.semaphore(name))

        w_hi = sb("w_hi", [P, CHUNKS, D], F32R)
        w_lo = sb("w_lo", [P, CHUNKS, D], F32R)
        wh_hi = sb("wh_hi", [P, TILES, D], F32R)
        wh_lo = sb("wh_lo", [P, TILES, D], F32R)
        adj_t = sb("adj_t", [P, TILES, N], F32R)
        xt_hi = sb("xt_hi", [P, 2, D], F32R)
        xt_lo = sb("xt_lo", [P, 2, D], F32R)
        x_in = sb("x_in", [P, 2, D], F32)
        adj_in = sb("adj_in", [P, N], I32)
        adj_h = sb("adj_h", [P, N], F16)
        adj_x = sb("adj_x", [P, TILES, P], F16)
        work = sb("work", [P, 4, D], F32)
        h_new = work[:, 0, :]
        rows = work[:, 1:3, :]
        exps = work[:, 3, :]
        planes = rows[:, 0, :].bitcast(U16)
        planes_t = exps.bitcast(U16)
        joined = rows[:, 1, :]
        count_scrap = sb("count_scrap", [P, N], BF16)
        a_sum = sb("a_sum", [P, D], F32)
        scrap = sb("scrap", [P, D], BF16)
        ident = sb("ident", [P, P], F32)
        score = sb("score", [P, TILES, H], F32)
        count = sb("count", [P, TILES], F32)
        absent = sb("absent", [P, TILES], F32)
        any_edge = sb("any_edge", [P, TILES], F32)
        all_edges = sb("all_edges", [P, TILES], F32)
        total = sb("total", [P, TILES, H], F32)
        top = total
        below = sb("below", [P, 2, TILES, H], F32)
        weight = below
        scale = sb("scale", [P, TILES, H], F32)
        row_sum = sb("row_sum", [P, 2], F32)
        neg_mean = sb("neg_mean", [P, 2], F32)
        sq_sum = sb("sq_sum", [P, 2], F32)
        variance = sb("variance", [P, 2], F32)
        rstd = sb("rstd", [P, 2], F32)
        shift = sb("shift", [P, 2], F32)
        per_feature = sb("per_feature", [P, 1], F32)
        eps = sb("eps", [P, 1], F32)
        minus_half = sb("minus_half", [P, 1], F32)

        acc = ps("acc", [P, BANKS, HALF], F32)
        xt_ps = ps("xt_ps", [P, CHUNKS, P], F32)

        w_loaded = [sem(f"w_loaded{s}") for s in range(4)]
        w_split = sem("w_split")
        a_loaded = sem("a_loaded")
        a_summed = sem("a_summed")
        w_rounded = sem("w_rounded")
        zeroed = sem("zeroed")
        consts_ready = sem("consts_ready")
        x_loaded = [sem(f"x_loaded{s}") for s in range(2)]
        x_turned = sem("x_turned")
        x_planed = sem("x_planed")
        planes_turned = sem("planes_turned")
        x_joined = sem("x_joined")
        xt_rounded = sem("xt_rounded")
        xt_split = sem("xt_split")
        adj_loaded = sem("adj_loaded")
        adj_cast = sem("adj_cast")
        adj_turned = sem("adj_turned")
        adj_t_ready = sem("adj_t_ready")
        adj_counted = sem("adj_counted")
        product_done = sem("product_done")
        bank_free = sem("bank_free")
        wh_rounded = sem("wh_rounded")
        wh_split = sem("wh_split")
        scored = sem("scored")
        exp_ready = sem("exp_ready")
        x_used = sem("x_used")
        row_summed = sem("row_summed")
        mean_ready = sem("mean_ready")
        squares_ready = sem("squares_ready")
        below_ready = sem("below_ready")
        weight_ready = sem("weight_ready")
        dve_step = sem("dve_step")
        pool_step = sem("pool_step")
        act_step = sem("act_step")
        rstd_ready = sem("rstd_ready")
        normed = sem("normed")
        stored = [sem(f"stored{s}") for s in range(2)]

        x_rows = x.rearrange("b n d -> (b n) d")
        adj_rows = adj.rearrange("b n d -> (b n) d")
        out_rows = out.rearrange("b n d -> (b n) d")
        w_rows = w.rearrange("o k n -> (o k) n")
        a_row = a.rearrange("o h f l -> (o l) (h f)")

        block = ctx.enter_context(nc.Block())

        @block.sync
        def _(sp):
            def load_x(b, t, slot):
                sp.dma_start(x_in[:, slot, :], x_rows[bass.ds(b * N + t * P, P), :]).then_inc(x_loaded[slot], 16)

            def load_adj(b, t):
                sp.dma_start(adj_in[:, :], adj_rows[bass.ds(b * N + t * P, P), :])\
                  .then_inc(adj_loaded, 16)

            def load_w(c):
                sp.dma_start(work[:, c % 4, :], w_rows[c * P:(c + 1) * P, :]).then_inc(w_loaded[c % 4], 16)

            def load_residual(b, i):
                load_x(b, i, (i + 1) % 2)

            def wait_residual(b, i):
                if i < 2:
                    sp.wait_ge(x_planed, BY_DMA * b + BY_DMA - 1 + i)
                else:
                    sp.wait_ge(x_used, TILES * b + i)

            load_x(0, 0, 0)
            for c in range(4):
                load_w(c)
            for c in range(4, CHUNKS):
                sp.wait_ge(w_split, c - 3)
                load_w(c)
            load_adj(0, 0)

            def graph(b, last):
                sp.wait_ge(x_turned, BY_PE * b + 1)
                load_x(b, 1, 0)
                sp.wait_ge(x_used, TILES * b + 1)
                load_x(b, 2, 1)
                for t in range(TILES):
                    sp.wait_ge(adj_cast, TILES * b + t + 1)
                    if t < TILES - 1:
                        load_adj(b, t + 1)
                    elif last:
                        wait_residual(b, 1)
                        load_residual(b, 1)
                    else:
                        load_adj(b + 1, 0)
                    sp.dma_start_transpose(adj_x[:, :, :], adj_h[:, :]).then_inc(adj_turned, 16)
                    if t > TILES - 3:
                        continue
                    sp.wait_ge(x_planed, BY_DMA * b + t + 1)
                    if t:
                        sp.wait_ge(x_joined, BY_DMA * b + t)
                    if t < TILES - 3:
                        load_x(b, t + 3, t % 2)
                    else:
                        load_residual(b, 0)
                    sp.dma_start_transpose(planes_t.rearrange("p (c q) -> p c q", q=P), planes)\
                      .then_inc(planes_turned, 16)
                for i in range(2 if last else 1, TILES - 1):
                    wait_residual(b, i)
                    load_residual(b, i)
                if not last:
                    sp.wait_ge(x_used, TILES * b + TILES - 1)
                    load_x(b + 1, 0, 0)
                sp.wait_ge(x_used, TILES * b + TILES)
                load_x(b, TILES - 1, 1)

            with sp.Fori(0, B - 1) as b:
                graph(b, False)
            graph(B - 1, True)

        @block.tensor
        def _(pe):
            def turn_x(loads):
                pe.wait_ge(x_loaded[0], 16 * loads)
                for c in range(CHUNKS):
                    last = nc.tensor.transpose(xt_ps[:, c, :], x_in[:, 0, c * P:(c + 1) * P], ident[:, :])
                last.then_inc(x_turned, 1)

            def make_wh(b, t, h):
                u = t * HALVES + h
                bank = acc[:, u % BANKS, :]
                cols = slice(h * HALF, (h + 1) * HALF)
                pe.wait_ge(bank_free, UNITS * b + u + 1)
                pe.wait_ge(xt_split, TILES * b + t + 1)
                for c in range(CHUNKS):
                    if u == 0:
                        pe.wait_ge(w_split, c + 1)
                    hi = xt_hi[:, t % 2, c * P:(c + 1) * P]
                    lo = xt_lo[:, t % 2, c * P:(c + 1) * P]
                    nc.tensor.matmul(bank, lo, w_hi[:, c, cols], start=(c == 0), stop=False)
                    nc.tensor.matmul(bank, hi, w_lo[:, c, cols], start=False, stop=False)
                    last = nc.tensor.matmul(bank, hi, w_hi[:, c, cols], start=False, stop=(c == CHUNKS - 1))
                last.then_inc(product_done, 1)

            def gather(b, i, h):
                u = SECOND + i * HALVES + h
                bank = acc[:, u % BANKS, :]
                cols = slice(h * HALF, (h + 1) * HALF)
                pe.wait_ge(adj_t_ready, TILES * b + i + 1)
                pe.wait_ge(bank_free, UNITS * b + u + 1)
                for j in range(TILES):
                    if i == 0:
                        pe.wait_ge(wh_split, SECOND * b + j * HALVES + h + 1)
                    edges = adj_t[:, i, j * P:(j + 1) * P]
                    nc.tensor.matmul(bank, edges, wh_lo[:, j, cols], start=(j == 0), stop=False)
                    last = nc.tensor.matmul(bank, edges, wh_hi[:, j, cols], start=False, stop=(j == TILES - 1))
                last.then_inc(product_done, 1)

            def graph(b, last):
                for t in range(TILES):
                    make_wh(b, t, 0)
                    if t == 0:
                        turn_x(TILES * b + 2)
                    make_wh(b, t, 1)
                for i in range(TILES):
                    gather(b, i, 0)
                    if i == TILES - 1 and not last:
                        turn_x(TILES * b + 9)
                    gather(b, i, 1)

            pe.wait_ge(consts_ready, 1)
            turn_x(1)
            with pe.Fori(0, B - 1) as b:
                graph(b, False)
            graph(B - 1, True)

        @block.scalar
        def _(act):
            def cast_adj(g, first=False):
                act.wait_ge(adj_loaded, 16 * (g + 1))
                if not first:
                    act.wait_ge(adj_counted, g)
                nc.scalar.activation(adj_h[:, :], adj_in[:, :], ACT.Copy).then_inc(adj_cast, 1)

            def round_xt(b, t):
                if t < 2:
                    act.wait_ge(x_turned, BY_PE * b + t + 1)
                    xt = xt_ps[:, :, :].rearrange("p c q -> p (c q)")
                else:
                    act.wait_ge(x_joined, BY_DMA * b + t - 1)
                    xt = joined
                nc.scalar.activation(xt_hi[:, t % 2, :], xt, ACT.Copy).then_inc(xt_rounded, 1)

            def plane_x(b, t, first):
                slot = (t - 1) % 2
                act.wait_ge(x_loaded[slot], 16 * (TILES * b + (t - 1) // 2 + (2 if slot == 0 else 1)))
                if t > 2:
                    act.wait_ge(planes_turned, 16 * (BY_DMA * b + t - 2))
                elif first:
                    act.wait_ge(a_summed, 1)
                else:
                    act.wait_ge(stored[0], STORES * b)
                nc.scalar.activation(planes.rearrange("p (s d) -> p s d", s=2),
                                     x_in[:, slot, :].bitcast(U16).rearrange("p (d s) -> p s d", s=2),
                                     ACT.Copy).then_inc(x_planed, 1)

            def round_wh(b, t, h):
                u = t * HALVES + h
                act.wait_ge(product_done, UNITS * b + u + 1)
                nc.scalar.activation(wh_hi[:, t, h * HALF:(h + 1) * HALF], acc[:, u % BANKS, :], ACT.Copy)\
                    .then_inc(wh_rounded, 1)

            def norm_squares(b, i):
                act.wait_ge(mean_ready, TILES * b + i + 1)
                nc.scalar.activation(scrap[:, :], rows[:, i % 2, :], ACT.Square, bias=neg_mean[:, i % 2:i % 2 + 1],
                                     accum_out=sq_sum[:, i % 2:i % 2 + 1]).then_inc(squares_ready, 1)

            def norm_store(b, i):
                s = i % 2
                act.wait_ge(rstd_ready, TILES * b + i + 1)
                nc.scalar.activation(rows[:, s, :], rows[:, s, :], ACT.Identity, bias=shift[:, s:s + 1],
                                     scale=rstd[:, s:s + 1]).then_inc(normed, 1)
                act.wait_ge(normed, TILES * b + i + 1)
                act.dma_start(out_rows[bass.ds(b * N + i * P, P), :], rows[:, s, :]).then_inc(stored[s], 16)

            def exp_neg_part(b, i, h):
                k = SECOND * b + 2 * i + h
                part = exps[:, h * HALF:(h + 1) * HALF]
                act.wait_ge(bank_free, UNITS * b + SECOND + 2 * i + h + 1 + BANKS)
                nc.scalar.activation(part, h_new[:, h * HALF:(h + 1) * HALF], ACT.Relu, scale=-1.0)\
                    .then_inc(act_step, 1)
                act.wait_ge(act_step, k + 1)
                nc.scalar.activation(part, part, ACT.Exp, scale=-1.0).then_inc(exp_ready, 1)

            def graph(b, first, last):
                for t in range(TILES):
                    if 0 < t < TILES - 2:
                        plane_x(b, t + 2, first)
                    if 0 < t < TILES - 1:
                        round_xt(b, t + 1)
                    round_wh(b, t, 0)
                    if t == 0:
                        round_xt(b, 1)
                        plane_x(b, 2, first)
                    if t == 0 and not first:
                        norm_store(b - 1, TILES - 1)
                    act.wait_ge(adj_turned, 16 * (TILES * b + t + 1))
                    nc.scalar.activation(adj_t[:, t, :], adj_x[:, :, :].rearrange("p j q -> p (j q)"), ACT.Copy)\
                        .then_inc(adj_t_ready, 1)
                    if t < TILES - 1 or not last:
                        cast_adj(TILES * b + t + 1)
                    round_wh(b, t, 1)
                act.wait_ge(below_ready, b + 1)
                nc.scalar.activation(weight[:, :, :, :], below[:, :, :, :], ACT.Exp).then_inc(weight_ready, 1)
                for i in range(TILES):
                    if i == TILES - 1 and not last:
                        round_xt(b + 1, 0)
                    exp_neg_part(b, i, 0)
                    exp_neg_part(b, i, 1)
                    if i:
                        norm_store(b, i - 1)
                    norm_squares(b, i)

            round_xt(0, 0)
            for c in range(CHUNKS):
                act.wait_ge(w_loaded[c % 4], 16 * (c // 4 + 1))
                nc.scalar.activation(w_hi[:, c, :], work[:, c % 4, :], ACT.Copy).then_inc(w_rounded, 1)
            act.wait_ge(w_split, CHUNKS - 1)
            act.dma_start(work[:, 1:3, :].rearrange("p t d -> p (t d)"),
                          a_row.to_broadcast([P, 2 * D])).then_inc(a_loaded, 16)
            cast_adj(0, first=True)
            graph(0, True, False)
            with act.Fori(1, B - 1) as b:
                graph(b, False, False)
            graph(B - 1, False, True)
            norm_store(B - 1, TILES - 1)
            for s in range(2):
                act.wait_ge(stored[s], 16 * B * TILES // 2)

        @block.vector
        def _(dve):
            def join_x(b, t, first):
                dve.wait_ge(planes_turned, 16 * (BY_DMA * b + t - 1))
                if t == 2 and not first:
                    dve.wait_ge(stored[1], STORES * b)
                nc.vector.tensor_copy(joined.bitcast(U16).rearrange("p (d s) -> p s d", s=2),
                                      planes_t.rearrange("p (s d) -> p s d", s=2)).then_inc(x_joined, 1)

            def split_xt(b, t):
                xt = xt_ps[:, :, :].rearrange("p c q -> p (c q)") if t < 2 else joined
                dve.wait_ge(xt_rounded, TILES * b + t + 1)
                nc.vector.tensor_tensor(xt_lo[:, t % 2, :], xt, xt_hi[:, t % 2, :].bitcast(F32), ALU.subtract)\
                    .then_inc(xt_split, 1)

            def count_edges(b, t):
                dve.wait_ge(adj_cast, TILES * b + t + 1)
                if t:
                    dve.wait_ge(adj_counted, TILES * b + t)
                nc.vector.tensor_scalar(count_scrap[:, :], adj_h[:, :], 0.0, None, ALU.not_equal, ALU.add,
                                        accum_out=count[:, t:t + 1]).then_inc(adj_counted, 1)

            def split_wh(b, t, h):
                u = t * HALVES + h
                cols = slice(h * HALF, (h + 1) * HALF)
                bank = acc[:, u % BANKS, :]
                dve.wait_ge(wh_rounded, SECOND * b + u + 1)
                nc.vector.tensor_tensor(wh_lo[:, t, cols], bank, wh_hi[:, t, cols].bitcast(F32), ALU.subtract)\
                    .then_inc(wh_split, 1)
                nc.vector.tensor_tensor(h_new[:, cols], bank, a_sum[:, cols], ALU.mult).then_inc(bank_free, 1)

            def score_wh(b, t, h):
                u = t * HALVES + h
                dve.wait_ge(bank_free, UNITS * b + u + 1 + BANKS)
                nc.vector.tensor_reduce(score[:, t, h * HH:(h + 1) * HH],
                                        h_new[:, h * HALF:(h + 1) * HALF].rearrange("p (h f) -> p h f", f=F),
                                        AX_X, ALU.add).then_inc(scored, 1)

            STEPS = 16

            def row_factors(b):
                done = [0]

                def step(ins):
                    done[0] += 1
                    ins.then_inc(dve_step, 1)
                    dve.wait_ge(dve_step, STEPS * b + done[0])

                def per_head(v):
                    return v[:, :].unsqueeze(2).to_broadcast([P, TILES, H])

                e_part, n_part = below[:, 0, :, :], below[:, 1, :, :]
                p, q = weight[:, 0, :, :], weight[:, 1, :, :]
                dve.wait_ge(scored, SECOND * (b + 1))
                dve.wait_ge(adj_counted, TILES * (b + 1))
                step(nc.vector.scalar_tensor_tensor(out=score[:, :, :], in0=score[:, :, :], scalar=ALPHA,
                                                    in1=score[:, :, :], op0=ALU.mult, op1=ALU.max))
                step(nc.vector.tensor_scalar(any_edge[:, :], count[:, :], 0.0, None, ALU.is_gt))
                step(nc.vector.tensor_scalar(all_edges[:, :], count[:, :], float(N), None, ALU.is_ge))
                step(nc.vector.tensor_scalar(absent[:, :], count[:, :], -1.0, float(N), ALU.mult, ALU.add))
                step(nc.vector.tensor_tensor(score[:, :, :], score[:, :, :], per_head(any_edge), ALU.mult))
                step(nc.vector.tensor_scalar(any_edge[:, :], any_edge[:, :], -NEG_INF, NEG_INF, ALU.mult, ALU.add))
                step(nc.vector.tensor_tensor(score[:, :, :], score[:, :, :], per_head(any_edge), ALU.add))
                step(nc.vector.tensor_scalar(all_edges[:, :], all_edges[:, :], LOWEST, NEG_INF, ALU.mult, ALU.add))
                step(nc.vector.tensor_tensor(top[:, :, :], score[:, :, :], per_head(all_edges), ALU.max))
                step(nc.vector.tensor_tensor(e_part, score[:, :, :], top[:, :, :], ALU.subtract))
                step(nc.vector.tensor_scalar(n_part, top[:, :, :], -1.0, NEG_INF, ALU.mult, ALU.add))
                nc.vector.tensor_scalar(n_part, n_part, 0.0, None, ALU.min).then_inc(below_ready, 1)
                dve.wait_ge(weight_ready, b + 1)
                step(nc.vector.tensor_tensor(total[:, :, :], p, per_head(count), ALU.mult))
                step(nc.vector.tensor_tensor(q, q, per_head(absent), ALU.mult))
                step(nc.vector.tensor_tensor(total[:, :, :], total[:, :, :], q, ALU.add))
                step(nc.vector.reciprocal(total[:, :, :], total[:, :, :]))
                nc.vector.tensor_tensor(scale[:, :, :], p, total[:, :, :], ALU.mult).then_inc(dve_step, 1)
                dve.wait_ge(dve_step, STEPS * b + done[0] + 1)
                assert done[0] + 1 == STEPS

            nc.vector.memset(neg_mean[:, :], 0.0).then_inc(x_used, 1)
            nc.vector.memset(per_feature[:, :], 1.0 / D)
            nc.vector.memset(eps[:, :], EPS)
            nc.vector.memset(minus_half[:, :], -0.5).then_inc(bank_free, BANKS)
            split_xt(0, 0)
            for c in range(CHUNKS):
                dve.wait_ge(w_rounded, c + 1)
                nc.vector.tensor_tensor(w_lo[:, c, :], work[:, c % 4, :], w_hi[:, c, :].bitcast(F32),
                                        ALU.subtract).then_inc(w_split, 1)
            dve.wait_ge(a_loaded, 16)
            pair = work[:, 1:3, :].rearrange("p t (h s f) -> p (t h) s f", s=2, f=F)
            nc.vector.tensor_tensor(a_sum[:, :].rearrange("p (h f) -> p h f", f=F), pair[:, :, 0, :],
                                    pair[:, :, 1, :], ALU.add).then_inc(a_summed, 1)
            dve.wait_ge(a_summed, 1)

            def graph(b, first, last):
                for t in range(TILES):
                    if 0 < t < TILES - 1:
                        join_x(b, t + 1, first)
                        split_xt(b, t + 1)
                    split_wh(b, t, 0)
                    score_wh(b, t, 0)
                    if t == 0:
                        split_xt(b, 1)
                    count_edges(b, t)
                    split_wh(b, t, 1)
                    score_wh(b, t, 1)
                row_factors(b)
                for i in range(TILES):
                    s = i % 2
                    for h in range(HALVES):
                        if h == 1 and i == TILES - 1 and not last:
                            split_xt(b + 1, 0)
                        u = SECOND + i * HALVES + h
                        dve.wait_ge(product_done, UNITS * b + u + 1)
                        nc.vector.tensor_tensor(
                            h_new[:, h * HALF:(h + 1) * HALF].rearrange("p (h f) -> p h f", f=F),
                            acc[:, u % BANKS, :].rearrange("p (h f) -> p h f", f=F),
                            scale[:, i, h * HH:(h + 1) * HH].unsqueeze(2).to_broadcast([P, HH, F]),
                            ALU.mult).then_inc(bank_free, 1)
                    n = TILES - 1 + i if i < TILES - 1 else 2 * TILES - 1
                    slot = n % 2
                    loads = TILES * b + n // 2 + (2 if n % 2 == 0 else 1)
                    dve.wait_ge(bank_free, UNITS * b + SECOND + 2 * i + 2 + BANKS)
                    dve.wait_ge(x_loaded[slot], 16 * loads)
                    if not first or i >= 2:
                        dve.wait_ge(stored[s], STORES * b + 16 * (i // 2))
                    nc.vector.scalar_tensor_tensor(out=rows[:, s, :], in0=h_new, scalar=0.0,
                                                   in1=x_in[:, slot, :], op0=ALU.max, op1=ALU.add)\
                        .then_inc(x_used, 1)
                    dve.wait_ge(x_used, TILES * b + i + 2)
                    dve.wait_ge(exp_ready, SECOND * b + 2 * i + 2)
                    nc.vector.scalar_tensor_tensor(out=rows[:, s, :], in0=exps, scalar=-1.0,
                                                   in1=rows[:, s, :], op0=ALU.add, op1=ALU.add,
                                                   accum_out=row_sum[:, s:s + 1]).then_inc(row_summed, 1)
                    dve.wait_ge(row_summed, TILES * b + i + 1)
                    nc.vector.tensor_scalar(neg_mean[:, s:s + 1], row_sum[:, s:s + 1], -1.0 / D, None, ALU.mult)\
                        .then_inc(mean_ready, 1)

            graph(0, True, False)
            with dve.Fori(1, B - 1) as b:
                graph(b, False, False)
            graph(B - 1, False, True)

        @block.gpsimd
        def _(pool):
            nc.gpsimd.memset(ident[:, :], 0.0).then_inc(zeroed, 1)
            pool.wait_ge(zeroed, 1)
            nc.gpsimd.affine_select(out=ident[:, :], in_=ident[:, :], compare_op=ALU.not_equal, fill=1.0,
                                    base=0, pattern=[[-1, P]], channel_multiplier=1).then_inc(consts_ready, 1)
            pool.wait_ge(bank_free, BANKS)

            def tile(g, s):
                one = slice(s, s + 1)
                pool.wait_ge(squares_ready, g + 1)
                nc.gpsimd.tensor_tensor(variance[:, one], sq_sum[:, one], per_feature[:, :], ALU.mult)\
                    .then_inc(pool_step, 1)
                pool.wait_ge(pool_step, 3 * g + 1)
                nc.gpsimd.tensor_tensor(variance[:, one], variance[:, one], eps[:, :], ALU.add)\
                    .then_inc(pool_step, 1)
                pool.wait_ge(pool_step, 3 * g + 2)
                nc.gpsimd.tensor_tensor(rstd[:, one], variance[:, one], minus_half[:, :], ALU.pow)\
                    .then_inc(pool_step, 1)
                pool.wait_ge(pool_step, 3 * g + 3)
                nc.gpsimd.tensor_tensor(shift[:, one], neg_mean[:, one], rstd[:, one], ALU.mult)\
                    .then_inc(rstd_ready, 1)

            with pool.Fori(0, B * TILES, 2) as g:
                tile(g, 0)
                tile(g + 1, 1)


def kernel(x, adj, L0_gnn_W, L0_gnn_a):
    import numpy as _np
    import concourse.bacc as _bacc
    from concourse import mybir as _mybir
    from concourse.bass_utils import run_bass_kernel_spmd as _run

    nc = _bacc.Bacc("TRN2", target_bir_lowering=False, num_devices=1, dynamic_dma_scratch_size=4096)
    arrays, args = {}, []
    for name, value in (("x", x), ("adj", adj), ("W", L0_gnn_W), ("a", L0_gnn_a)):
        v = _np.ascontiguousarray(value)
        arrays[f"in_{name}"] = v
        args.append(nc.dram_tensor(f"in_{name}", v.shape, _mybir.dt.from_np(v.dtype), kind="ExternalInput").ap())
    args.append(nc.dram_tensor("out", arrays["in_x"].shape, _mybir.dt.float32, kind="ExternalOutput").ap())
    gat_resnorm_kernel(nc, *args)
    r = _run(nc, [arrays], core_ids=[0])
    return r.results[0]["out"]
```
